# Optimizing a Trainium2 kernel written in Bass

```python
import numpy as np
import jax
import jax.numpy as jnp

def _softmax(x, axis=-1):
    return jax.nn.softmax(x, axis=axis)

def _gelu(x):
    return jax.nn.gelu(x, approximate=True)

def _silu(x):
    return jax.nn.silu(x)

def _sigmoid(x):
    return jax.nn.sigmoid(x)

def _layernorm(x, axis=-1, eps=1e-05):
    m = jnp.mean(x, axis=axis, keepdims=True)
    v = jnp.var(x, axis=axis, keepdims=True)
    return (x - m) / jnp.sqrt(v + eps)

def _scatter_add(tgt, idx, src, axis=0):
    return tgt.at[idx].add(src)

def _segment_sum(src, seg, n):
    return jax.ops.segment_sum(src, seg, n)
kernel_name = 'mk_dlrm_tower_d1_rec_r8_5e0371'

def setup_inputs(seed: int=0):
    np.random.seed(seed)
    _w = jnp.asarray

    def _rec_inputs():
        import jax
        import jax.numpy as jnp
        _tk = jax.random.key(seed)
        ids = jnp.stack([jax.random.randint(jax.random.fold_in(_tk, 200 + f), (512,), 0, v, jnp.int32) for f, v in enumerate([1000, 125000, 1250, 1250, 12500, 1250, 12500, 1250, 12500, 12500, 1000, 1000, 1250, 12500, 1250, 12500, 1000, 1250, 1000, 12500, 12500, 1250, 1250, 1000, 1250, 1000])], axis=1)
        tbl_0 = 0.05 * jax.random.normal(jax.random.fold_in(_tk, 500 + 0), (1000, 128), jnp.float32)
        tbl_1 = 0.05 * jax.random.normal(jax.random.fold_in(_tk, 500 + 1), (125000, 128), jnp.float32)
        tbl_2 = 0.05 * jax.random.normal(jax.random.fold_in(_tk, 500 + 2), (1250, 128), jnp.float32)
        tbl_3 = 0.05 * jax.random.normal(jax.random.fold_in(_tk, 500 + 3), (1250, 128), jnp.float32)
        tbl_4 = 0.05 * jax.random.normal(jax.random.fold_in(_tk, 500 + 4), (12500, 128), jnp.float32)
        tbl_5 = 0.05 * jax.random.normal(jax.random.fold_in(_tk, 500 + 5), (1250, 128), jnp.float32)
        tbl_6 = 0.05 * jax.random.normal(jax.random.fold_in(_tk, 500 + 6), (12500, 128), jnp.float32)
        tbl_7 = 0.05 * jax.random.normal(jax.random.fold_in(_tk, 500 + 7), (1250, 128), jnp.float32)
        tbl_8 = 0.05 * jax.random.normal(jax.random.fold_in(_tk, 500 + 8), (12500, 128), jnp.float32)
        tbl_9 = 0.05 * jax.random.normal(jax.random.fold_in(_tk, 500 + 9), (12500, 128), jnp.float32)
        tbl_10 = 0.05 * jax.random.normal(jax.random.fold_in(_tk, 500 + 10), (1000, 128), jnp.float32)
        tbl_11 = 0.05 * jax.random.normal(jax.random.fold_in(_tk, 500 + 11), (1000, 128), jnp.float32)
        tbl_12 = 0.05 * jax.random.normal(jax.random.fold_in(_tk, 500 + 12), (1250, 128), jnp.float32)
        tbl_13 = 0.05 * jax.random.normal(jax.random.fold_in(_tk, 500 + 13), (12500, 128), jnp.float32)
        tbl_14 = 0.05 * jax.random.normal(jax.random.fold_in(_tk, 500 + 14), (1250, 128), jnp.float32)
        tbl_15 = 0.05 * jax.random.normal(jax.random.fold_in(_tk, 500 + 15), (12500, 128), jnp.float32)
        tbl_16 = 0.05 * jax.random.normal(jax.random.fold_in(_tk, 500 + 16), (1000, 128), jnp.float32)
        tbl_17 = 0.05 * jax.random.normal(jax.random.fold_in(_tk, 500 + 17), (1250, 128), jnp.float32)
        tbl_18 = 0.05 * jax.random.normal(jax.random.fold_in(_tk, 500 + 18), (1000, 128), jnp.float32)
        tbl_19 = 0.05 * jax.random.normal(jax.random.fold_in(_tk, 500 + 19), (12500, 128), jnp.float32)
        tbl_20 = 0.05 * jax.random.normal(jax.random.fold_in(_tk, 500 + 20), (12500, 128), jnp.float32)
        tbl_21 = 0.05 * jax.random.normal(jax.random.fold_in(_tk, 500 + 21), (1250, 128), jnp.float32)
        tbl_22 = 0.05 * jax.random.normal(jax.random.fold_in(_tk, 500 + 22), (1250, 128), jnp.float32)
        tbl_23 = 0.05 * jax.random.normal(jax.random.fold_in(_tk, 500 + 23), (1000, 128), jnp.float32)
        tbl_24 = 0.05 * jax.random.normal(jax.random.fold_in(_tk, 500 + 24), (1250, 128), jnp.float32)
        tbl_25 = 0.05 * jax.random.normal(jax.random.fold_in(_tk, 500 + 25), (1000, 128), jnp.float32)
        _rk = jax.random.fold_in(_tk, 7)
        r_dense_features = -0.000520686 + 1.00062 * jax.random.normal(jax.random.fold_in(_rk, 101), (512, 128), jnp.float32)
        W_top1 = 0.0405887 * jax.random.normal(jax.random.fold_in(_tk, 801), (607, 512), jnp.float32)
        W_top2 = 0.0441942 * jax.random.normal(jax.random.fold_in(_tk, 802), (512, 256), jnp.float32)
        W_top3 = 0.0625 * jax.random.normal(jax.random.fold_in(_tk, 803), (256, 1), jnp.float32)
        b_top1 = jnp.zeros((512,), jnp.float32)
        b_top2 = jnp.zeros((256,), jnp.float32)
        return (r_dense_features, ids, tbl_0, tbl_1, tbl_2, tbl_3, tbl_4, tbl_5, tbl_6, tbl_7, tbl_8, tbl_9, tbl_10, tbl_11, tbl_12, tbl_13, tbl_14, tbl_15, tbl_16, tbl_17, tbl_18, tbl_19, tbl_20, tbl_21, tbl_22, tbl_23, tbl_24, tbl_25, W_top1, b_top1, W_top2, b_top2, W_top3)
    r_dense_features, ids, tbl_0, tbl_1, tbl_2, tbl_3, tbl_4, tbl_5, tbl_6, tbl_7, tbl_8, tbl_9, tbl_10, tbl_11, tbl_12, tbl_13, tbl_14, tbl_15, tbl_16, tbl_17, tbl_18, tbl_19, tbl_20, tbl_21, tbl_22, tbl_23, tbl_24, tbl_25, W_top1, b_top1, W_top2, b_top2, W_top3 = _rec_inputs()

    def _L0_rec_setup():
        import jax, jax.numpy as jnp
        import numpy as np
        NUM_SPARSE = 26
        EMBED_DIM = 128
        BATCH = 2048
        key = jax.random.key(seed)
        k1, k2 = jax.random.split(key)
        dense_features = jax.random.normal(k1, (BATCH, EMBED_DIM), dtype=jnp.float32)
        sparse_features = jax.random.normal(k2, (BATCH, NUM_SPARSE, EMBED_DIM), dtype=jnp.float32)
        return {'dense_features': dense_features, 'sparse_features': sparse_features}
    _L0_rec_all = _L0_rec_setup()
    _L0_rec_in = {k: v for k, v in _L0_rec_all.items() if k in ()}
    del _L0_rec_all
    return {'r_dense_features': r_dense_features, 'ids': ids, 'tbl_0': tbl_0, 'tbl_1': tbl_1, 'tbl_2': tbl_2, 'tbl_3': tbl_3, 'tbl_4': tbl_4, 'tbl_5': tbl_5, 'tbl_6': tbl_6, 'tbl_7': tbl_7, 'tbl_8': tbl_8, 'tbl_9': tbl_9, 'tbl_10': tbl_10, 'tbl_11': tbl_11, 'tbl_12': tbl_12, 'tbl_13': tbl_13, 'tbl_14': tbl_14, 'tbl_15': tbl_15, 'tbl_16': tbl_16, 'tbl_17': tbl_17, 'tbl_18': tbl_18, 'tbl_19': tbl_19, 'tbl_20': tbl_20, 'tbl_21': tbl_21, 'tbl_22': tbl_22, 'tbl_23': tbl_23, 'tbl_24': tbl_24, 'tbl_25': tbl_25, 'W_top1': W_top1, 'b_top1': b_top1, 'W_top2': W_top2, 'b_top2': b_top2, 'W_top3': W_top3}

def reference(r_dense_features, ids, tbl_0, tbl_1, tbl_2, tbl_3, tbl_4, tbl_5, tbl_6, tbl_7, tbl_8, tbl_9, tbl_10, tbl_11, tbl_12, tbl_13, tbl_14, tbl_15, tbl_16, tbl_17, tbl_18, tbl_19, tbl_20, tbl_21, tbl_22, tbl_23, tbl_24, tbl_25, W_top1, b_top1, W_top2, b_top2, W_top3):
    import jax
    import jax.numpy as jnp

    def _L0_rec_ref(dense_features, sparse_features):
        import jax, jax.numpy as jnp
        import numpy as np
        NUM_SPARSE = 26
        EMBED_DIM = 128
        BATCH = 2048
        F = NUM_SPARSE + 1
        combined = jnp.concatenate([dense_features[:, None, :], sparse_features], axis=1)
        interactions = jnp.einsum('bfd,bgd->bfg', combined, combined)
        iu, ju = jnp.triu_indices(F, k=1)
        interactions_flat = interactions[:, iu, ju]
        return jnp.concatenate([dense_features, interactions_flat], axis=1)
    e = jnp.stack([tbl_0[ids[:, 0]], tbl_1[ids[:, 1]], tbl_2[ids[:, 2]], tbl_3[ids[:, 3]], tbl_4[ids[:, 4]], tbl_5[ids[:, 5]], tbl_6[ids[:, 6]], tbl_7[ids[:, 7]], tbl_8[ids[:, 8]], tbl_9[ids[:, 9]], tbl_10[ids[:, 10]], tbl_11[ids[:, 11]], tbl_12[ids[:, 12]], tbl_13[ids[:, 13]], tbl_14[ids[:, 14]], tbl_15[ids[:, 15]], tbl_16[ids[:, 16]], tbl_17[ids[:, 17]], tbl_18[ids[:, 18]], tbl_19[ids[:, 19]], tbl_20[ids[:, 20]], tbl_21[ids[:, 21]], tbl_22[ids[:, 22]], tbl_23[ids[:, 23]], tbl_24[ids[:, 24]], tbl_25[ids[:, 25]]], axis=1)
    z = _L0_rec_ref(r_dense_features, e)
    z = z.reshape(z.shape[0], -1)
    h = jnp.concatenate([z, r_dense_features], axis=1)
    h = jnp.maximum(h @ W_top1 + b_top1, 0.0)
    h = jnp.maximum(h @ W_top2 + b_top2, 0.0)
    y = h @ W_top3
    return y

_drawn_inputs = setup_inputs


def setup_inputs(seed=0):
    import zlib

    import numpy as np

    out = dict(_drawn_inputs(seed))
    spreads = {'b_top1': (0.0, 0.1), 'b_top2': (0.0, 0.1)}
    factors = {}
    for name, (base, spread) in spreads.items():
        noise = np.random.default_rng([zlib.crc32(name.encode()), seed]).standard_normal(out[name].shape)
        drawn = base * np.exp(spread * noise) if base else spread * noise
        out[name] = jnp.asarray(drawn.astype(out[name].dtype))
    for name, factor in factors.items():
        out[name] = (out[name] * factor).astype(out[name].dtype)
    return out
```

```python
from contextlib import ExitStack

import concourse.bass as bass
from concourse import mybir

F32 = mybir.dt.float32
F32R = mybir.dt.float32r
I32 = mybir.dt.int32
U32 = mybir.dt.uint32
ALU = mybir.AluOpType
ACT = mybir.ActivationFunctionType

P = 128
N_TABLES = 26
N_FEATURES = N_TABLES + 1
PAD = 32
QUARTERS = 4
JQ = P // QUARTERS
GATHER_GROUP = 4

ONE_HOT_TABLES = [0, 10, 11, 16, 18, 23]
GATHERED_TABLES = [n for n in range(N_TABLES) if n not in ONE_HOT_TABLES]
N_ONE_HOT = len(ONE_HOT_TABLES)
N_GATHERED = len(GATHERED_TABLES)
SLOTS = [0] + [n + 1 for n in ONE_HOT_TABLES] + [n + 1 for n in GATHERED_TABLES]

LANES = 4
BLOCKS = -(-N_FEATURES // LANES)
BLOCK_ROWS = [min(LANES * c + LANES - 1, N_FEATURES - 1) for c in range(BLOCKS)]
BLOCK_AT = [sum(BLOCK_ROWS[:c]) for c in range(BLOCKS)]
PAIR_ROWS = sum(BLOCK_ROWS)


def dlrm_tower(nc, dense, ids_gather, ids_one_hot, tables, w_dense, w_pairs, b1, w2, b2, w3, out):
    batch = dense.shape[0]
    tiles = batch // P
    rows = tables[ONE_HOT_TABLES[0]].shape[0]
    KR = 125
    chunks = rows // KR
    hidden1 = w_dense.shape[2]
    hidden2 = w2.shape[1]
    n1, n2 = hidden1 // P, hidden2 // P
    assert all(tables[n].shape[0] == rows for n in ONE_HOT_TABLES) and rows == KR * chunks

    moved = 1 + N_GATHERED
    groups = [range(a, min(a + GATHER_GROUP, moved)) for a in range(0, moved, GATHER_GROUP)]
    NG = len(groups)
    act_groups = len(range(0, NG, 2))
    dve_groups = NG - act_groups
    assert NG == N_ONE_HOT
    HALF = JQ // 2

    def slot(m):
        return 0 if m == 0 else N_ONE_HOT + m

    with ExitStack() as ctx:
        def sb(name, shape, dt=F32):
            return ctx.enter_context(nc.sbuf_tensor(name, shape, dt))

        def psum(name, shape):
            return ctx.enter_context(nc.psum_tensor(name, shape, F32))

        def sem(name):
            return ctx.enter_context(nc.semaphore(name))

        ident = sb("ident", [P, P])
        row_id = sb("row_id", [KR, chunks])
        idx = sb("idx", [P, tiles, N_GATHERED], I32)
        ids_all = sb("ids_all", [KR, N_ONE_HOT, batch], I32)
        table = sb("table", [KR, N_ONE_HOT, chunks, P])
        table_hi = [sb(f"table_hi{i}", [KR, chunks, P], F32R) for i in range(2)]
        table_lo = [sb(f"table_lo{i}", [KR, chunks, P], F32R) for i in range(2)]
        one_hot = [sb(f"one_hot{i}", [KR, chunks, batch], F32R) for i in range(2)]
        looked_up = sb("looked_up", [P, N_ONE_HOT, batch])
        e = sb("e", [P, moved, P])
        eT = sb("eT", [P, P, PAD])
        gram = sb("gram", [P, LANES * BLOCKS, JQ])
        pairs_t = sb("pairs_t", [P, QUARTERS, PAIR_ROWS])
        pairs = sb("pairs", [PAIR_ROWS, LANES, P])
        wd = sb("wd", [P, 2, hidden1])
        wd_sum = sb("wd_sum", [P, hidden1])
        wp = sb("wp", [PAIR_ROWS, LANES, hidden1])
        w2s = sb("w2s", [P, n1, hidden2])
        w3s = sb("w3s", [P, n2])
        b1s = sb("b1s", [P, n1])
        b2s = sb("b2s", [P, n2])
        h1 = sb("h1", [P, n1, P])
        h2 = sb("h2", [P, n2, P])
        y = sb("y", [1, batch])

        ps_x = [psum(f"ps_x{i}", [P, GATHER_GROUP, P]) for i in range(2)]
        ps_g = [psum(f"ps_g{i}", [P, 512]) for i in range(2)]
        ps_t = [psum(f"ps_t{i}", [P, 4, P]) for i in range(2)]
        ps_h = [psum(f"ps_h{i}", [P, n1 // 2, P]) for i in range(2)]
        ps_z = [ps_g[i][:, 0:2 * P].rearrange("p (q s) -> p q s", q=2) for i in range(2)]
        ps_h2 = [ps_t[i][:, 0, :] for i in range(n2)]
        ps_y = ps_g[1][0:1, 0:P]

        s_idx = sem("s_idx")
        s_ids_all = [sem(f"s_ids_all{i}") for i in range(N_ONE_HOT)]
        s_table = [sem(f"s_table{i}") for i in range(N_ONE_HOT)]
        s_dense = sem("s_dense")
        s_wd = sem("s_wd")
        s_w = sem("s_w")
        s_wd_sum = sem("s_wd_sum")
        s_eT_read = sem("s_eT_read")
        s_gathered = [sem(f"s_gathered{i}") for i in range(NG)]
        s_const = sem("s_const")
        s_hi = sem("s_hi")
        s_lo = sem("s_lo")
        s_one_hot = sem("s_one_hot")
        s_lookup = sem("s_lookup")
        s_looked_up = sem("s_looked_up")
        s_zero = sem("s_zero")
        s_moved = sem("s_moved")
        s_x_act = sem("s_x_act")
        s_x_dve = sem("s_x_dve")
        s_slots = sem("s_slots")
        s_gram = sem("s_gram")
        s_gram_act = sem("s_gram_act")
        s_gram_dve = sem("s_gram_dve")
        s_turn = sem("s_turn")
        s_turn_act = sem("s_turn_act")
        s_turn_dve = sem("s_turn_dve")
        s_pairs = sem("s_pairs")
        s_pairs_act = sem("s_pairs_act")
        s_pairs_dve = sem("s_pairs_dve")
        s_h1 = sem("s_h1")
        s_h1_act = sem("s_h1_act")
        s_h1_dve = sem("s_h1_dve")
        s_h2 = sem("s_h2")
        s_h2_act = sem("s_h2_act")
        s_h2_dve = sem("s_h2_dve")
        s_y = sem("s_y")
        s_y_row = sem("s_y_row")
        s_out = sem("s_out")

        block = ctx.enter_context(nc.Block())

        @block.sync
        def _(sp):
            for i, n in enumerate(ONE_HOT_TABLES):
                sp.dma_start(ids_all[:, i, :], ids_one_hot[i].partition_broadcast(KR)).then_inc(s_ids_all[i], 16)
                sp.dma_start(table[:, i], tables[n].rearrange("(p c) d -> p c d", c=chunks)).then_inc(s_table[i], 16)
            sp.dma_start(wd[:], w_dense.rearrange("s p n -> p s n")).then_inc(s_wd, 16)
            sp.dma_start(wp[:], w_pairs.rearrange("a p n -> p a n")).then_inc(s_w, 16)
            sp.dma_start(w2s[:], w2.rearrange("(c p) n -> p c n", p=P)).then_inc(s_w, 16)
            sp.dma_start(w3s[:], w3).then_inc(s_w, 16)
            sp.dma_start(b1s[:], b1).then_inc(s_w, 16)
            sp.dma_start(b2s[:], b2).then_inc(s_w, 16)
            for t in range(1, tiles):
                sp.wait_ge(s_moved, NG * (t - 1) + 1)
                sp.dma_start(e[:, 0, :], dense[t * P:(t + 1) * P, :]).then_inc(s_dense, 16)
            sp.wait_ge(s_y_row, tiles)
            sp.dma_start(out.rearrange("b o -> o b"), y[:]).then_inc(s_out, 16)
            sp.wait_ge(s_out, 16)

        @block.gpsimd
        def _(pool):
            pool.memset(ident[:], 0.0).then_inc(s_const, 1)
            pool.iota(row_id[:], [[1, chunks]], base=0, channel_multiplier=chunks,
                      allow_small_or_imprecise_dtypes=True).then_inc(s_const, 1)
            pool.wait_ge(s_const, 1)
            pool.affine_select(out=ident[:], in_=ident[:], compare_op=ALU.not_equal, fill=1.0, base=0,
                               pattern=[[-1, P]], channel_multiplier=1).then_inc(s_const, 1)
            pool.wait_ge(s_idx, 16)
            for t in range(tiles):
                for g, group in enumerate(groups):
                    if t:
                        pool.wait_ge(s_moved, NG * (t - 1) + g + 1)
                    for m in group:
                        if m:
                            pool.indirect_dma_start(
                                e[:, m, :], None, tables[GATHERED_TABLES[m - 1]],
                                bass.IndirectOffsetOnAxis(ap=idx[:, t, m - 1:m].bitcast(U32), axis=0),
                            ).then_inc(s_gathered[g], 16)

        @block.scalar
        def _(act):
            def to_eT(g):
                group = groups[g]
                parts = [(0, 0, 1), (slot(1), 1, len(group))] if g == 0 else [(slot(group[0]), 0, len(group))]
                for at, a, b in parts:
                    last = act.copy(eT[:, :, at:at + b - a].rearrange("p s f -> p f s"), ps_x[0][:, a:b, :])
                last.then_inc(s_x_act, 1)

            def tile(t, more):
                act.wait_ge(s_gram, 2 * t + 1)
                act.copy(gram[:, 0:N_FEATURES, 0:HALF].rearrange("p g j -> p j g"),
                         ps_g[0][:, 0:HALF * N_FEATURES].rearrange("p (j g) -> p j g", g=N_FEATURES)).then_inc(s_gram_act, 1)
                act.wait_ge(s_turn, 2 * t + 1)
                for c in range(4):
                    last = act.copy(pairs_t[:, :, BLOCK_AT[c]:BLOCK_AT[c] + BLOCK_ROWS[c]],
                                    ps_t[0][:, c, :].rearrange("p (q f) -> p q f", f=PAD)[:, :, 0:BLOCK_ROWS[c]])
                last.then_inc(s_turn_act, 1)
                act.wait_ge(s_pairs, t + 1)
                act.copy(pairs[:, :, 0:2 * JQ].rearrange("p a (q j) -> p q a j", j=JQ),
                         ps_z[0][0:PAIR_ROWS].rearrange("p q (a j) -> p q a j", j=JQ)).then_inc(s_pairs_act, 1)
                if more:
                    act.wait_ge(s_eT_read, t + 1)
                    act.wait_ge(s_moved, NG * (t + 1) + 1)
                    to_eT(0)
                act.wait_ge(s_h1, 2 * t + 1)
                for n in range(n1 // 2):
                    act.activation(h1[:, n, :], ps_h[0][:, n, :], ACT.Relu, bias=b1s[:, n:n + 1]).then_inc(s_h1_act, 1)
                for n in range(0, n2, 2):
                    act.wait_ge(s_h2, n2 * t + n + 1)
                    act.activation(h2[:, n, :], ps_h2[n], ACT.Relu, bias=b2s[:, n:n + 1]).then_inc(s_h2_act, 1)
                if more:
                    for g in range(2, NG, 2):
                        act.wait_ge(s_moved, NG * (t + 1) + g + 1)
                        to_eT(g)

            act.dma_start(idx[:], ids_gather.rearrange("t p f -> p t f")).then_inc(s_idx, 16)
            act.dma_start(e[:, 0, :], dense[0:P, :]).then_inc(s_dense, 16)
            for n in range(N_ONE_HOT):
                act.wait_ge(s_table[n], 16)
                if n >= 2:
                    act.wait_ge(s_lookup, n - 1)
                act.activation(table_hi[n % 2][:], table[:, n], ACT.Copy).then_inc(s_hi, 1)
                if n:
                    act.wait_ge(s_lookup, n)
                    act.copy(looked_up[:, n - 1, :], ps_g[(n - 1) % 2][:]).then_inc(s_looked_up, 1)
                if n % 2:
                    act.wait_ge(s_moved, n)
                    to_eT(n - 1)
            act.wait_ge(s_lookup, N_ONE_HOT)
            act.copy(looked_up[:, N_ONE_HOT - 1, :], ps_g[(N_ONE_HOT - 1) % 2][:]).then_inc(s_looked_up, 1)
            act.wait_ge(s_w, 16 * 5)
            with act.Fori(0, tiles - 1) as t:
                tile(t, True)
            tile(tiles - 1, False)

        @block.vector
        def _(dve):
            def to_eT(g):
                group = groups[g]
                at = slot(group[0])
                dve.tensor_copy(eT[:, :, at:at + len(group)].rearrange("p s f -> p f s"),
                                ps_x[1][:, 0:len(group), :]).then_inc(s_x_dve, 1)

            def one_hot_slots(t):
                dve.tensor_copy(eT[:, :, 1:1 + N_ONE_HOT].rearrange("p s f -> p f s"),
                                looked_up[:, :, bass.ts(t, P)]).then_inc(s_slots, 1)

            def tile(t, more):
                dve.wait_ge(s_gram, 2 * t + 2)
                dve.tensor_copy(gram[:, 0:N_FEATURES, HALF:JQ].rearrange("p g j -> p j g"),
                                ps_g[1][:, 0:HALF * N_FEATURES].rearrange("p (j g) -> p j g", g=N_FEATURES)).then_inc(s_gram_dve, 1)
                dve.wait_ge(s_turn, 2 * t + 2)
                for c in range(4, BLOCKS):
                    last = dve.tensor_copy(pairs_t[:, :, BLOCK_AT[c]:BLOCK_AT[c] + BLOCK_ROWS[c]],
                                           ps_t[1][:, c - 4, :].rearrange("p (q f) -> p q f", f=PAD)[:, :, 0:BLOCK_ROWS[c]])
                last.then_inc(s_turn_dve, 1)
                dve.wait_ge(s_pairs, t + 1)
                dve.tensor_copy(pairs[:, :, 2 * JQ:4 * JQ].rearrange("p a (q j) -> p q a j", j=JQ),
                                ps_z[1][0:PAIR_ROWS].rearrange("p q (a j) -> p q a j", j=JQ)).then_inc(s_pairs_dve, 1)
                if more:
                    dve.wait_ge(s_eT_read, t + 1)
                    one_hot_slots(t + 1)
                    dve.wait_ge(s_moved, NG * (t + 1) + 2)
                    to_eT(1)
                dve.wait_ge(s_h1, 2 * t + 2)
                for n in range(n1 // 2, n1):
                    dve.tensor_scalar(h1[:, n, :], ps_h[1][:, n - n1 // 2, :], b1s[:, n:n + 1], 0.0, ALU.add, ALU.max).then_inc(s_h1_dve, 1)
                for n in range(1, n2, 2):
                    dve.wait_ge(s_h2, n2 * t + n + 1)
                    dve.tensor_scalar(h2[:, n, :], ps_h2[n], b2s[:, n:n + 1], 0.0, ALU.add, ALU.max).then_inc(s_h2_dve, 1)
                dve.wait_ge(s_y, t + 1)
                dve.tensor_copy(y[0:1, bass.ts(t, P)], ps_y).then_inc(s_y_row, 1)
                if more:
                    for g in range(3, NG, 2):
                        dve.wait_ge(s_moved, NG * (t + 1) + g + 1)
                        to_eT(g)

            dve.memset(eT[:, :, N_FEATURES:PAD], 0.0).then_inc(s_zero, 1)
            dve.memset(gram[:, N_FEATURES:LANES * BLOCKS, :], 0.0).then_inc(s_zero, 1)
            dve.wait_ge(s_const, 2)
            for n in range(N_ONE_HOT):
                dve.wait_ge(s_ids_all[n], 16)
                if n >= 2:
                    dve.wait_ge(s_lookup, n - 1)
                for c in range(chunks):
                    last = dve.tensor_scalar(one_hot[n % 2][:, c, :], ids_all[:, n, :], row_id[:, c:c + 1], None,
                                             ALU.is_equal)
                last.then_inc(s_one_hot, 1)
                dve.wait_ge(s_hi, n + 1)
                dve.tensor_tensor(table_lo[n % 2][:], table[:, n], table_hi[n % 2][:].bitcast(F32),
                                  ALU.subtract).then_inc(s_lo, 1)
                if n and n % 2 == 0:
                    dve.wait_ge(s_moved, n)
                    to_eT(n - 1)
            dve.wait_ge(s_wd, 16)
            dve.tensor_tensor(wd_sum[:], wd[:, 0, :], wd[:, 1, :], ALU.add).then_inc(s_wd_sum, 1)
            dve.wait_ge(s_moved, NG)
            to_eT(NG - 1)
            dve.wait_ge(s_looked_up, N_ONE_HOT)
            one_hot_slots(0)
            dve.wait_ge(s_w, 16 * 5)
            with dve.Fori(0, tiles - 1) as t:
                tile(t, True)
            tile(tiles - 1, False)

        @block.tensor
        def _(pe):
            def move(t, g):
                if g == 0:
                    pe.wait_ge(s_dense, 16 * t + 16)
                pe.wait_ge(s_gathered[g], 16 * len([m for m in groups[g] if m]) * (t + 1))
                for i, m in enumerate(groups[g]):
                    last = pe.transpose(ps_x[g % 2][:, i, :], e[:, m, :], ident[:])
                last.then_inc(s_moved, 1)

            def move_next(t, g):
                if g % 2 == 0:
                    pe.wait_ge(s_x_act, act_groups * (t + 1) + g // 2)
                else:
                    pe.wait_ge(s_x_dve, dve_groups * (t + 1) + g // 2)
                move(t + 1, g)

            def tile(t, more):
                pe.wait_ge(s_x_act, act_groups * (t + 1))
                pe.wait_ge(s_x_dve, dve_groups * (t + 1))
                pe.wait_ge(s_slots, t + 1)
                for j in range(JQ):
                    at = (j % HALF) * N_FEATURES
                    for q in range(QUARTERS):
                        s = q * JQ + j
                        last = pe.matmul(ps_g[j // HALF][q * PAD:(q + 1) * PAD, at:at + N_FEATURES], eT[:, s, :],
                                         eT[:, s, 0:N_FEATURES], start=True, stop=True, tile_position=(0, q * PAD))
                    if j % HALF == HALF - 1:
                        last.then_inc(s_gram, 1)
                for n in range(n1):
                    last = pe.matmul(ps_h[n // 2][:, n % 2, :], wd_sum[:, n * P:(n + 1) * P], eT[:, :, 0],
                              start=(n % 2 == 0), stop=False, skip_group_check=True)
                last.then_inc(s_eT_read, 1)
                pe.wait_ge(s_gram_act, t + 1)
                pe.wait_ge(s_gram_dve, t + 1)
                for c in range(BLOCKS):
                    last = pe.transpose(ps_t[c // 4][:, c % 4, :],
                                        gram[:, LANES * c:LANES * c + LANES, :].rearrange("p g j -> p (g j)"), ident[:])
                    if c in (3, BLOCKS - 1):
                        last.then_inc(s_turn, 1)
                if more:
                    move_next(t, 0)
                pe.wait_ge(s_turn_act, t + 1)
                pe.wait_ge(s_turn_dve, t + 1)
                for q in range(QUARTERS):
                    last = pe.transpose(ps_z[q // 2][0:PAIR_ROWS, q % 2, :], pairs_t[:, q, :], ident[:])
                last.then_inc(s_pairs, 1)
                if more:
                    move_next(t, 1)
                pe.wait_ge(s_pairs_act, t + 1)
                pe.wait_ge(s_pairs_dve, t + 1)
                for n in range(n1):
                    for a in range(LANES):
                        last = pe.matmul(ps_h[n // 2][:, n % 2, :], wp[:, a, n * P:(n + 1) * P], pairs[:, a, :],
                                         start=False, stop=(a == LANES - 1), skip_group_check=True)
                    if n % 2:
                        last.then_inc(s_h1, 1)
                for n in range(n2):
                    for k in range(n1):
                        if n == 0 and k < n1 // 2:
                            pe.wait_ge(s_h1_act, (n1 // 2) * t + k + 1)
                        elif n == 0:
                            pe.wait_ge(s_h1_dve, (n1 // 2) * t + k - n1 // 2 + 1)
                        last = pe.matmul(ps_h2[n], w2s[:, k, n * P:(n + 1) * P], h1[:, k, :],
                                         start=(k == 0), stop=(k == n1 - 1))
                    last.then_inc(s_h2, 1)
                pe.wait_ge(s_h2_act, t + 1)
                pe.wait_ge(s_h2_dve, t + 1)
                for n in range(n2):
                    last = pe.matmul(ps_y, w3s[:, n:n + 1], h2[:, n, :], start=(n == 0), stop=(n == n2 - 1))
                last.then_inc(s_y, 1)
                if more:
                    for g in range(2, NG):
                        move_next(t, g)
                    pe.wait_ge(s_y_row, t + 1)

            pe.wait_ge(s_const, 3)
            for n in range(N_ONE_HOT):
                pe.wait_ge(s_one_hot, n + 1)
                pe.wait_ge(s_lo, n + 1)
                if n >= 2:
                    pe.wait_ge(s_looked_up, n - 1)
                for i, half in enumerate((table_hi, table_lo)):
                    for c in range(chunks):
                        last = pe.matmul(ps_g[n % 2][:], half[n % 2][:, c, :], one_hot[n % 2][:, c, :],
                                         start=(i == 0 and c == 0), stop=(i == 1 and c == chunks - 1))
                last.then_inc(s_lookup, 1)
                if n >= 2:
                    pe.wait_ge(s_x_act if n % 2 == 0 else s_x_dve, n // 2)
                move(0, n)
            pe.wait_ge(s_looked_up, N_ONE_HOT)
            pe.wait_ge(s_wd_sum, 1)
            pe.wait_ge(s_w, 16 * 5)
            pe.wait_ge(s_zero, 2)
            with pe.Fori(0, tiles - 1) as t:
                tile(t, True)
            tile(tiles - 1, False)


def kernel(**inputs):
    import numpy as np
    import concourse.bacc as bacc
    from concourse.bass_utils import run_bass_kernel_spmd

    nc = bacc.Bacc("TRN2", target_bir_lowering=False, num_devices=1)
    given = {name: np.asarray(a) for name, a in inputs.items()}
    batch = given["ids"].shape[0]

    w1 = given["W_top1"]
    zero_row = w1.shape[0]
    row_of, at = {}, P
    for i in range(N_FEATURES):
        for j in range(i + 1, N_FEATURES):
            row_of[i, j] = at
            at += 1
    order = np.full((LANES, PAIR_ROWS), zero_row)
    for a in range(LANES):
        for c in range(BLOCKS):
            g = LANES * c + a
            for f in range(min(g, N_FEATURES - 1) if g < N_FEATURES else 0):
                order[a, BLOCK_AT[c] + f] = row_of[min(SLOTS[f], SLOTS[g]), max(SLOTS[f], SLOTS[g])]
    w1_padded = np.concatenate([w1, np.zeros((1, w1.shape[1]), w1.dtype)])

    arrays = {
        "dense": given["r_dense_features"],
        "ids_gather": given["ids"][:, GATHERED_TABLES].reshape(batch // P, P, N_GATHERED),
        "ids_one_hot": given["ids"].T[ONE_HOT_TABLES],
        "w_dense": np.stack([w1[:P], w1[-P:]]),
        "w_pairs": w1_padded[order],
        "b1": given["b_top1"].reshape(-1, P).T,
        "w2": given["W_top2"],
        "b2": given["b_top2"].reshape(-1, P).T,
        "w3": given["W_top3"].reshape(-1, P).T,
    }
    arrays.update({f"tbl_{n}": given[f"tbl_{n}"] for n in range(N_TABLES)})
    arrays = {name: np.ascontiguousarray(a) for name, a in arrays.items()}
    ap = {name: nc.dram_tensor(name, a.shape, mybir.dt.from_np(a.dtype), kind="ExternalInput").ap()
          for name, a in arrays.items()}
    out = nc.dram_tensor("y_out", (batch, 1), F32, kind="ExternalOutput").ap()
    dlrm_tower(nc, ap["dense"], ap["ids_gather"], ap["ids_one_hot"], [ap[f"tbl_{n}"] for n in range(N_TABLES)],
               ap["w_dense"], ap["w_pairs"], ap["b1"], ap["w2"], ap["b2"], ap["w3"], out)
    r = run_bass_kernel_spmd(nc, [arrays], core_ids=[0])
    return r.results[0]["y_out"]
```

```python
from contextlib import ExitStack

import concourse.bass as bass
from concourse import mybir

F32 = mybir.dt.float32
F32R = mybir.dt.float32r
I32 = mybir.dt.int32
U32 = mybir.dt.uint32
ALU = mybir.AluOpType
ACT = mybir.ActivationFunctionType

P = 128
N_TABLES = 26
N_FEATURES = N_TABLES + 1
PAD = 32
QUARTERS = 4
JQ = P // QUARTERS
GATHER_GROUP = 4

ONE_HOT_TABLES = [0, 10, 11, 16, 18, 23]
GATHERED_TABLES = [n for n in range(N_TABLES) if n not in ONE_HOT_TABLES]
N_ONE_HOT = len(ONE_HOT_TABLES)
N_GATHERED = len(GATHERED_TABLES)
SLOTS = [0] + [n + 1 for n in ONE_HOT_TABLES] + [n + 1 for n in GATHERED_TABLES]

LANES = 4
BLOCKS = -(-N_FEATURES // LANES)
BLOCK_ROWS = [min(LANES * c + LANES - 1, N_FEATURES - 1) for c in range(BLOCKS)]
BLOCK_AT = [sum(BLOCK_ROWS[:c]) for c in range(BLOCKS)]
PAIR_ROWS = sum(BLOCK_ROWS)


def dlrm_tower(nc, dense, ids_gather, ids_one_hot, tables, w_dense, w_pairs, b1, w2, b2, w3, out):
    batch = dense.shape[0]
    tiles = batch // P
    rows = tables[ONE_HOT_TABLES[0]].shape[0]
    KR = 125
    chunks = rows // KR
    SPREAD = KR // 16 * 16
    hidden1 = w_dense.shape[2]
    hidden2 = w2.shape[1]
    n1, n2 = hidden1 // P, hidden2 // P
    assert n1 == 4 and n2 == 2 and tiles == 4
    assert all(tables[n].shape[0] == rows for n in ONE_HOT_TABLES) and rows == KR * chunks

    moved = 1 + N_GATHERED
    groups = [range(a, min(a + GATHER_GROUP, moved)) for a in range(0, moved, GATHER_GROUP)]
    NG = len(groups)
    SPAN = 2 * P
    units = [(n, h) for h in range(batch // SPAN) for n in range(N_ONE_HOT)]
    OH_RING = 4

    JOBS = [
        [[("look", 0)], [("move", 0), ("look", 1)], [("look", 2), ("move", 1)], [("look", 3)],
         [("move", 2), ("look", 4), ("move", 3), ("look", 5), ("look", 6), ("look", 7), ("move", 4), ("move", 5)]],
        [[("look", 8)], [("look", 9)], [("move", 0), ("look", 10), ("move", 1)], [("look", 11)],
         [("move", 2), ("move", 3), ("move", 4), ("move", 5)]],
    ] + [[[], [("move", 0)], [("move", 1)], [("move", 2)], [("move", 3), ("move", 4)], [("move", 5)]]
         for _ in range(tiles - 2)]
    PARTS = 5
    numbered, count = [], 0
    for parts in JOBS:
        numbered.append([])
        for part in parts:
            numbered[-1].append([(count + i, (count + i) % 2, kind, what) for i, (kind, what) in enumerate(part)])
            count += len(part)
    job_number = {(at if kind == "move" else 0, kind, what): k
                  for at, parts in enumerate(numbered) for part in parts for k, _, kind, what in part}

    def move_job(t, g):
        return job_number[t, "move", g]

    def look_job(u):
        return job_number[0, "look", u]

    def in_bank(bank, jobs):
        return (jobs + 1 - bank) // 2

    def jobs_until(t):
        return sum(len(part) for parts in JOBS[:t + 1] for part in parts)

    HALF = JQ // 2

    def slot(m):
        return 0 if m == 0 else N_ONE_HOT + m

    with ExitStack() as ctx:
        def sb(name, shape, dt=F32):
            return ctx.enter_context(nc.sbuf_tensor(name, shape, dt))

        def psum(name, shape):
            return ctx.enter_context(nc.psum_tensor(name, shape, F32))

        def sem(name):
            return ctx.enter_context(nc.semaphore(name))

        ident = sb("ident", [P, P])
        row_id = sb("row_id", [KR, chunks])
        idx = sb("idx", [P, tiles, N_GATHERED], I32)
        ids_all = sb("ids_all", [P, N_ONE_HOT, batch], I32)
        table = sb("table", [KR, N_ONE_HOT, chunks, P])
        table_hi = [sb(f"table_hi{n}", [KR, chunks, P], F32R) for n in range(N_ONE_HOT)]
        table_lo = [sb(f"table_lo{n}", [KR, chunks, P], F32R) for n in range(N_ONE_HOT)]
        one_hot = [sb(f"one_hot{i}", [KR, chunks, SPAN], F32R) for i in range(OH_RING)]
        looked_up = sb("looked_up", [P, N_ONE_HOT, batch])
        e = sb("e", [P, moved, P])
        eT = sb("eT", [P, P, PAD])
        gram = sb("gram", [P, LANES * BLOCKS, JQ])
        pairs_t = sb("pairs_t", [P, QUARTERS, PAIR_ROWS])
        pairs = sb("pairs", [PAIR_ROWS, LANES, P])
        wd = sb("wd", [P, 2, hidden1])
        wd_sum = sb("wd_sum", [P, hidden1])
        wp = sb("wp", [PAIR_ROWS, LANES, hidden1])
        w2s = sb("w2s", [P, n1, hidden2])
        w3s = sb("w3s", [P, n2])
        b1s = sb("b1s", [P, n1])
        b2s = sb("b2s", [P, n2])
        h1 = sb("h1", [P, n1, P])
        h2 = sb("h2", [P, n2, P])
        y = sb("y", [1, batch])

        ps_x = [psum(f"ps_x{i}", [P, GATHER_GROUP, P]) for i in range(2)]
        ps_g = [psum(f"ps_g{i}", [P, 512]) for i in range(2)]
        ps_t = [psum(f"ps_t{i}", [P, 4, P]) for i in range(2)]
        ps_h = [psum(f"ps_h{i}", [P, 4, P]) for i in range(2)]
        ps_h2 = [ps_h[i][:, 2, :] for i in range(n2)]
        ps_y = ps_h[1][0:1, 3, :]
        ps_z = [ps_g[i][:, 0:2 * P].rearrange("p (q s) -> p q s", q=2) for i in range(2)]

        s_idx = sem("s_idx")
        s_ids_all = [sem(f"s_ids_all{i}") for i in range(N_ONE_HOT)]
        s_table = [sem(f"s_table{i}") for i in range(N_ONE_HOT)]
        s_dense = sem("s_dense")
        s_wd = sem("s_wd")
        s_w = sem("s_w")
        s_wd_sum = sem("s_wd_sum")
        s_eT_read = sem("s_eT_read")
        s_gathered = [sem(f"s_gathered{i}") for i in range(NG)]
        s_const = sem("s_const")
        s_hi = sem("s_hi")
        s_lo = sem("s_lo")
        s_one_hot = sem("s_one_hot")
        s_zero = sem("s_zero")
        s_x = sem("s_x")
        s_emptied = [sem(f"s_emptied{i}") for i in range(2)]
        s_slots = sem("s_slots")
        s_gram = sem("s_gram")
        s_gram_act = sem("s_gram_act")
        s_gram_dve = sem("s_gram_dve")
        s_turn = sem("s_turn")
        s_turn_act = sem("s_turn_act")
        s_turn_dve = sem("s_turn_dve")
        s_pairs = sem("s_pairs")
        s_pairs_act = sem("s_pairs_act")
        s_pairs_dve = sem("s_pairs_dve")
        s_h1 = sem("s_h1")
        s_h1_act = sem("s_h1_act")
        s_h1_dve = sem("s_h1_dve")
        s_h2 = sem("s_h2")
        s_h2_act = sem("s_h2_act")
        s_h2_dve = sem("s_h2_dve")
        s_y = sem("s_y")
        s_y_row = sem("s_y_row")
        s_out = sem("s_out")

        def copies(kind, what, bank):
            if kind == "look":
                n, h = units[what]
                return [(looked_up[:, n, h * SPAN:(h + 1) * SPAN], bank[:, 0:2, :].rearrange("p a s -> p (a s)"))]
            group = groups[what]
            parts = [(0, 0, 1), (slot(1), 1, len(group))] if what == 0 else [(slot(group[0]), 0, len(group))]
            return [(eT[:, :, at:at + b - a].rearrange("p s f -> p f s"), bank[:, a:b, :]) for at, a, b in parts]

        block = ctx.enter_context(nc.Block())

        @block.sync
        def _(sp):
            for i, n in enumerate(ONE_HOT_TABLES):
                if i >= 3:
                    sp.wait_ge(s_lo, i - 2)
                sp.dma_start(ids_all[:, i, :], ids_one_hot[i].partition_broadcast(P)).then_inc(s_ids_all[i], 16)
                rows_of = tables[n].rearrange("(p c) d -> p c d", c=chunks)
                sp.dma_start(table[0:SPREAD, i], rows_of[0:SPREAD]).then_inc(s_table[i], 16)
                sp.dma_start(table[SPREAD:KR, i], rows_of[SPREAD:KR]).then_inc(s_table[i], 16)
            sp.wait_ge(s_lo, N_ONE_HOT - 2)
            sp.dma_start(wd[:], w_dense.rearrange("s p n -> p s n")).then_inc(s_wd, 16)
            sp.wait_ge(s_lo, N_ONE_HOT)
            sp.dma_start(wp[:], w_pairs.rearrange("a p n -> p a n")).then_inc(s_w, 16)
            sp.dma_start(w2s[:], w2.rearrange("(c p) n -> p c n", p=P)).then_inc(s_w, 16)
            sp.dma_start(w3s[:], w3).then_inc(s_w, 16)
            sp.dma_start(b1s[:], b1).then_inc(s_w, 16)
            sp.dma_start(b2s[:], b2).then_inc(s_w, 16)
            for t in range(1, tiles):
                sp.wait_ge(s_x, move_job(t - 1, 0) + 1)
                sp.dma_start(e[:, 0, :], dense[t * P:(t + 1) * P, :]).then_inc(s_dense, 16)
            sp.wait_ge(s_y_row, tiles)
            sp.dma_start(out.rearrange("b o -> o b"), y[:]).then_inc(s_out, 16)
            sp.wait_ge(s_out, 16)

        @block.gpsimd
        def _(pool):
            pool.memset(ident[:], 0.0).then_inc(s_const, 1)
            pool.iota(row_id[:], [[1, chunks]], base=0, channel_multiplier=chunks,
                      allow_small_or_imprecise_dtypes=True).then_inc(s_const, 1)
            pool.wait_ge(s_const, 1)
            pool.affine_select(out=ident[:], in_=ident[:], compare_op=ALU.not_equal, fill=1.0, base=0,
                               pattern=[[-1, P]], channel_multiplier=1).then_inc(s_const, 1)
            pool.wait_ge(s_idx, 16)
            for t in range(tiles):
                for g, group in enumerate(groups):
                    if t:
                        pool.wait_ge(s_x, move_job(t - 1, g) + 1)
                    for m in group:
                        if m:
                            pool.indirect_dma_start(
                                e[:, m, :], None, tables[GATHERED_TABLES[m - 1]],
                                bass.IndirectOffsetOnAxis(ap=idx[:, t, m - 1:m].bitcast(U32), axis=0),
                            ).then_inc(s_gathered[g], 16)

        @block.scalar
        def _(act):
            def empty(t, part, banks=(0,)):
                for k, bank, kind, what in numbered[t][part]:
                    if bank in banks:
                        act.wait_ge(s_x, k + 1)
                        if kind == "move" and t:
                            act.wait_ge(s_eT_read, t)
                        for out, in_ in copies(kind, what, ps_x[bank]):
                            last = act.copy(out, in_)
                        last.then_inc(s_emptied[bank], 1)

            def gram_out(t):
                act.wait_ge(s_gram, 2 * t + 1)
                act.copy(gram[:, 0:N_FEATURES, 0:HALF].rearrange("p g j -> p j g"),
                         ps_g[0][:, 0:HALF * N_FEATURES].rearrange("p (j g) -> p j g", g=N_FEATURES)).then_inc(s_gram_act, 1)

            def turn_out(t):
                act.wait_ge(s_turn, 2 * t + 1)
                for c in range(4):
                    last = act.copy(pairs_t[:, :, BLOCK_AT[c]:BLOCK_AT[c] + BLOCK_ROWS[c]],
                                    ps_t[0][:, c, :].rearrange("p (q f) -> p q f", f=PAD)[:, :, 0:BLOCK_ROWS[c]])
                last.then_inc(s_turn_act, 1)

            def pairs_out(t):
                act.wait_ge(s_pairs, t + 1)
                act.copy(pairs[:, :, 0:2 * JQ].rearrange("p a (q j) -> p q a j", j=JQ),
                         ps_z[0][0:PAIR_ROWS].rearrange("p q (a j) -> p q a j", j=JQ)).then_inc(s_pairs_act, 1)

            def layer1_out(t):
                act.wait_ge(s_h1, 2 * t + 1)
                for n in range(n1 // 2):
                    act.activation(h1[:, n, :], ps_h[0][:, n, :], ACT.Relu, bias=b1s[:, n:n + 1]).then_inc(s_h1_act, 1)

            def layer2_out(t):
                act.wait_ge(s_h2, 2 * t + 1)
                act.activation(h2[:, 0, :], ps_h2[0], ACT.Relu, bias=b2s[:, 0:1]).then_inc(s_h2_act, 1)

            def high_halves(n):
                act.wait_ge(s_table[n], 32)
                act.activation(table_hi[n][:], table[:, n], ACT.Copy).then_inc(s_hi, 1)

            act.dma_start(idx[:], ids_gather.rearrange("t p f -> p t f")).then_inc(s_idx, 16)
            act.dma_start(e[:, 0, :], dense[0:P, :]).then_inc(s_dense, 16)
            high_halves(0)
            for part in range(PARTS):
                if part + 1 < N_ONE_HOT:
                    high_halves(part + 1)
                empty(0, part, (0, 1))

            gram_out(0)
            empty(1, 0)
            turn_out(0)
            empty(1, 1)
            pairs_out(0)
            for part in range(2, PARTS):
                empty(1, part)
            act.wait_ge(s_w, 16 * 5)
            gram_out(1)
            layer1_out(0)
            turn_out(1)
            layer2_out(0)
            pairs_out(1)
            empty(2, 1)
            empty(2, 2)
            layer1_out(1)
            empty(2, 3)
            layer2_out(1)
            empty(2, 4)
            for t in range(2, tiles):
                more = t + 1 < tiles
                empty(t, 5)
                gram_out(t)
                turn_out(t)
                pairs_out(t)
                if more:
                    empty(t + 1, 1)
                    empty(t + 1, 2)
                layer1_out(t)
                if more:
                    empty(t + 1, 3)
                layer2_out(t)
                if more:
                    empty(t + 1, 4)

        @block.vector
        def _(dve):
            def empty(t, part):
                for k, bank, kind, what in numbered[t][part]:
                    if bank == 1:
                        dve.wait_ge(s_x, k + 1)
                        if kind == "move":
                            dve.wait_ge(s_eT_read, t)
                        for out, in_ in copies(kind, what, ps_x[1]):
                            last = dve.tensor_copy(out, in_)
                        last.then_inc(s_emptied[1], 1)

            def one_hot_rows(u):
                n, h = units[u]
                if u >= OH_RING:
                    dve.wait_ge(s_x, look_job(u - OH_RING) + 1)
                for c in range(chunks):
                    last = dve.tensor_scalar(one_hot[u % OH_RING][:, c, :], ids_all[0:KR, n, h * SPAN:(h + 1) * SPAN],
                                             row_id[:, c:c + 1], None, ALU.is_equal)
                last.then_inc(s_one_hot, 1)

            def one_hot_slots(t):
                done = look_job(N_ONE_HOT * (t * P // SPAN + 1) - 1) + 1
                for bank in range(2):
                    dve.wait_ge(s_emptied[bank], in_bank(bank, done))
                if t:
                    dve.wait_ge(s_eT_read, t)
                dve.tensor_copy(eT[:, :, 1:1 + N_ONE_HOT].rearrange("p s f -> p f s"),
                                looked_up[:, :, t * P:(t + 1) * P]).then_inc(s_slots, 1)

            def gram_out(t):
                dve.wait_ge(s_gram, 2 * t + 2)
                dve.tensor_copy(gram[:, 0:N_FEATURES, HALF:JQ].rearrange("p g j -> p j g"),
                                ps_g[1][:, 0:HALF * N_FEATURES].rearrange("p (j g) -> p j g", g=N_FEATURES)).then_inc(s_gram_dve, 1)

            def turn_out(t):
                dve.wait_ge(s_turn, 2 * t + 2)
                for c in range(4, BLOCKS):
                    last = dve.tensor_copy(pairs_t[:, :, BLOCK_AT[c]:BLOCK_AT[c] + BLOCK_ROWS[c]],
                                           ps_t[1][:, c - 4, :].rearrange("p (q f) -> p q f", f=PAD)[:, :, 0:BLOCK_ROWS[c]])
                last.then_inc(s_turn_dve, 1)

            def pairs_out(t):
                dve.wait_ge(s_pairs, t + 1)
                dve.tensor_copy(pairs[:, :, 2 * JQ:4 * JQ].rearrange("p a (q j) -> p q a j", j=JQ),
                                ps_z[1][0:PAIR_ROWS].rearrange("p q (a j) -> p q a j", j=JQ)).then_inc(s_pairs_dve, 1)

            def layer1_out(t):
                dve.wait_ge(s_h1, 2 * t + 2)
                for n in range(n1 // 2, n1):
                    dve.tensor_scalar(h1[:, n, :], ps_h[1][:, n - n1 // 2, :], b1s[:, n:n + 1], 0.0,
                                      ALU.add, ALU.max).then_inc(s_h1_dve, 1)

            def layer2_out(t):
                dve.wait_ge(s_h2, 2 * t + 2)
                dve.tensor_scalar(h2[:, 1, :], ps_h2[1], b2s[:, 1:2], 0.0, ALU.add, ALU.max).then_inc(s_h2_dve, 1)

            def output_out(t):
                dve.wait_ge(s_y, t + 1)
                dve.tensor_copy(y[0:1, t * P:(t + 1) * P], ps_y).then_inc(s_y_row, 1)

            dve.memset(eT[:, :, N_FEATURES:PAD], 0.0).then_inc(s_zero, 1)
            dve.memset(gram[:, N_FEATURES:LANES * BLOCKS, :], 0.0).then_inc(s_zero, 1)
            dve.wait_ge(s_const, 2)
            for n in range(N_ONE_HOT):
                dve.wait_ge(s_ids_all[n], 16)
                one_hot_rows(n)
                dve.wait_ge(s_hi, n + 1)
                dve.tensor_tensor(table_lo[n][:], table[:, n], table_hi[n][:].bitcast(F32),
                                  ALU.subtract).then_inc(s_lo, 1)
            one_hot_rows(6)
            one_hot_rows(7)
            one_hot_slots(0)
            dve.wait_ge(s_wd, 16)
            dve.tensor_tensor(wd_sum[:], wd[:, 0, :], wd[:, 1, :], ALU.add).then_inc(s_wd_sum, 1)
            one_hot_rows(8)
            one_hot_rows(9)

            gram_out(0)
            empty(1, 0)
            turn_out(0)
            one_hot_rows(10)
            empty(1, 1)
            pairs_out(0)
            one_hot_rows(11)
            empty(1, 2)
            empty(1, 3)
            one_hot_slots(1)
            empty(1, 4)
            dve.wait_ge(s_w, 16 * 5)
            gram_out(1)
            layer1_out(0)
            turn_out(1)
            layer2_out(0)
            pairs_out(1)
            output_out(0)
            empty(2, 1)
            empty(2, 2)
            layer1_out(1)
            empty(2, 3)
            layer2_out(1)
            one_hot_slots(2)
            empty(2, 4)
            for t in range(2, tiles):
                more = t + 1 < tiles
                empty(t, 5)
                output_out(t - 1)
                gram_out(t)
                turn_out(t)
                pairs_out(t)
                if more:
                    empty(t + 1, 1)
                    empty(t + 1, 2)
                layer1_out(t)
                if more:
                    empty(t + 1, 3)
                layer2_out(t)
                if more:
                    one_hot_slots(t + 1)
                    empty(t + 1, 4)
            output_out(tiles - 1)

        @block.tensor
        def _(pe):
            def run(t, part):
                for k, bank, kind, what in numbered[t][part]:
                    if k >= 2:
                        pe.wait_ge(s_emptied[bank], in_bank(bank, k))
                    if kind == "look":
                        n, _ = units[what]
                        pe.wait_ge(s_one_hot, what + 1)
                        pe.wait_ge(s_lo, min(what + 1, N_ONE_HOT))
                        for half in (table_hi, table_lo):
                            for c in range(chunks):
                                last = pe.matmul(ps_x[bank][:, 0:2, :].rearrange("p a s -> p (a s)"), half[n][:, c, :],
                                                 one_hot[what % OH_RING][:, c, :],
                                                 start=(half is table_hi and c == 0),
                                                 stop=(half is table_lo and c == chunks - 1))
                    else:
                        if what == 0:
                            pe.wait_ge(s_dense, 16 * t + 16)
                        pe.wait_ge(s_gathered[what], 16 * len([m for m in groups[what] if m]) * (t + 1))
                        for i, m in enumerate(groups[what]):
                            last = pe.transpose(ps_x[bank][:, i, :], e[:, m, :], ident[:])
                    last.then_inc(s_x, 1)

            def grams(t, half):
                if half == 0:
                    for bank in range(2):
                        pe.wait_ge(s_emptied[bank], in_bank(bank, jobs_until(t)))
                    pe.wait_ge(s_slots, t + 1)
                    if t:
                        pe.wait_ge(s_pairs_act, t)
                        pe.wait_ge(s_pairs_dve, t)
                for j in range(HALF):
                    for q in range(QUARTERS):
                        s = q * JQ + half * HALF + j
                        last = pe.matmul(ps_g[half][q * PAD:(q + 1) * PAD, j * N_FEATURES:(j + 1) * N_FEATURES],
                                         eT[:, s, :], eT[:, s, 0:N_FEATURES], start=True, stop=True,
                                         tile_position=(0, q * PAD))
                last.then_inc(s_gram, 1)

            def dense_part(t, half):
                if t and half == 1:
                    pe.wait_ge(s_y_row, t)
                for n in range(2 * half, 2 * half + 2):
                    last = pe.matmul(ps_h[n // 2][:, n % 2, :], wd_sum[:, n * P:(n + 1) * P], eT[:, :, 0],
                                     start=(n % 2 == 0), stop=False, skip_group_check=True)
                if half == 1:
                    last.then_inc(s_eT_read, 1)

            def turn(t):
                pe.wait_ge(s_gram_act, t + 1)
                pe.wait_ge(s_gram_dve, t + 1)
                for c in range(BLOCKS):
                    last = pe.transpose(ps_t[c // 4][:, c % 4, :],
                                        gram[:, LANES * c:LANES * c + LANES, :].rearrange("p g j -> p (g j)"), ident[:])
                    if c in (3, BLOCKS - 1):
                        last.then_inc(s_turn, 1)

            def pair_turn(t):
                pe.wait_ge(s_turn_act, t + 1)
                pe.wait_ge(s_turn_dve, t + 1)
                for q in range(QUARTERS):
                    last = pe.transpose(ps_z[q // 2][0:PAIR_ROWS, q % 2, :], pairs_t[:, q, :], ident[:])
                last.then_inc(s_pairs, 1)

            def layer1(t, half):
                if half == 0:
                    pe.wait_ge(s_pairs_act, t + 1)
                    pe.wait_ge(s_pairs_dve, t + 1)
                for n in range(2 * half, 2 * half + 2):
                    for a in range(LANES):
                        last = pe.matmul(ps_h[half][:, n % 2, :], wp[:, a, n * P:(n + 1) * P], pairs[:, a, :],
                                         start=False, stop=(a == LANES - 1), skip_group_check=True)
                last.then_inc(s_h1, 1)

            def layer2(t, n):
                for k in range(n1):
                    if n == 0 and k == 0:
                        pe.wait_ge(s_h1_act, 2 * t + 2)
                    elif n == 0 and k >= 2:
                        pe.wait_ge(s_h1_dve, 2 * t + k - 1)
                    last = pe.matmul(ps_h2[n], w2s[:, k, n * P:(n + 1) * P], h1[:, k, :],
                                     start=(k == 0), stop=(k == n1 - 1))
                last.then_inc(s_h2, 1)

            def layer3(t):
                pe.wait_ge(s_h2_act, t + 1)
                pe.wait_ge(s_h2_dve, t + 1)
                for n in range(n2):
                    last = pe.matmul(ps_y, w3s[:, n:n + 1], h2[:, n, :], start=(n == 0), stop=(n == n2 - 1))
                last.then_inc(s_y, 1)

            pe.wait_ge(s_const, 3)
            for part in range(PARTS):
                run(0, part)
            pe.wait_ge(s_wd_sum, 1)
            pe.wait_ge(s_zero, 2)
            grams(0, 0)
            grams(0, 1)
            dense_part(0, 0)
            dense_part(0, 1)
            run(1, 0)
            turn(0)
            run(1, 1)
            pair_turn(0)
            for part in range(2, PARTS):
                run(1, part)
            pe.wait_ge(s_w, 16 * 5)
            grams(1, 0)
            layer1(0, 0)
            grams(1, 1)
            layer1(0, 1)
            turn(1)
            layer2(0, 0)
            layer2(0, 1)
            pair_turn(1)
            layer3(0)
            dense_part(1, 0)
            dense_part(1, 1)
            run(2, 1)
            run(2, 2)
            layer1(1, 0)
            layer1(1, 1)
            run(2, 3)
            layer2(1, 0)
            layer2(1, 1)
            run(2, 4)
            for t in range(2, tiles):
                more = t + 1 < tiles
                run(t, 5)
                layer3(t - 1)
                grams(t, 0)
                grams(t, 1)
                dense_part(t, 0)
                turn(t)
                dense_part(t, 1)
                pair_turn(t)
                if more:
                    run(t + 1, 1)
                    run(t + 1, 2)
                layer1(t, 0)
                layer1(t, 1)
                if more:
                    run(t + 1, 3)
                layer2(t, 0)
                layer2(t, 1)
                if more:
                    run(t + 1, 4)
            layer3(tiles - 1)


def kernel(**inputs):
    import numpy as np
    import concourse.bacc as bacc
    from concourse.bass_utils import run_bass_kernel_spmd

    nc = bacc.Bacc("TRN2", target_bir_lowering=False, num_devices=1)
    given = {name: np.asarray(a) for name, a in inputs.items()}
    batch = given["ids"].shape[0]

    w1 = given["W_top1"]
    zero_row = w1.shape[0]
    row_of, at = {}, P
    for i in range(N_FEATURES):
        for j in range(i + 1, N_FEATURES):
            row_of[i, j] = at
            at += 1
    order = np.full((LANES, PAIR_ROWS), zero_row)
    for a in range(LANES):
        for c in range(BLOCKS):
            g = LANES * c + a
            for f in range(min(g, N_FEATURES - 1) if g < N_FEATURES else 0):
                order[a, BLOCK_AT[c] + f] = row_of[min(SLOTS[f], SLOTS[g]), max(SLOTS[f], SLOTS[g])]
    w1_padded = np.concatenate([w1, np.zeros((1, w1.shape[1]), w1.dtype)])

    arrays = {
        "dense": given["r_dense_features"],
        "ids_gather": given["ids"][:, GATHERED_TABLES].reshape(batch // P, P, N_GATHERED),
        "ids_one_hot": given["ids"].T[ONE_HOT_TABLES],
        "w_dense": np.stack([w1[:P], w1[-P:]]),
        "w_pairs": w1_padded[order],
        "b1": given["b_top1"].reshape(-1, P).T,
        "w2": given["W_top2"],
        "b2": given["b_top2"].reshape(-1, P).T,
        "w3": given["W_top3"].reshape(-1, P).T,
    }
    arrays.update({f"tbl_{n}": given[f"tbl_{n}"] for n in range(N_TABLES)})
    arrays = {name: np.ascontiguousarray(a) for name, a in arrays.items()}
    ap = {name: nc.dram_tensor(name, a.shape, mybir.dt.from_np(a.dtype), kind="ExternalInput").ap()
          for name, a in arrays.items()}
    out = nc.dram_tensor("y_out", (batch, 1), F32, kind="ExternalOutput").ap()
    dlrm_tower(nc, ap["dense"], ap["ids_gather"], ap["ids_one_hot"], [ap[f"tbl_{n}"] for n in range(N_TABLES)],
               ap["w_dense"], ap["w_pairs"], ap["b1"], ap["w2"], ap["b2"], ap["w3"], out)
    r = run_bass_kernel_spmd(nc, [arrays], core_ids=[0])
    return r.results[0]["y_out"]
```

```python
from contextlib import ExitStack

import concourse.bass as bass
from concourse import mybir

F32 = mybir.dt.float32
F32R = mybir.dt.float32r
I32 = mybir.dt.int32
U32 = mybir.dt.uint32
ALU = mybir.AluOpType
ACT = mybir.ActivationFunctionType

P = 128
N_TABLES = 26
N_FEATURES = N_TABLES + 1
PAD = 32
QUARTERS = 4
JQ = P // QUARTERS
GATHER_GROUP = 4

ONE_HOT_TABLES = [0, 10, 11, 16, 18, 23]
LATE_TABLE = 25
GATHERED_TABLES = [LATE_TABLE] + [n for n in range(N_TABLES) if n not in ONE_HOT_TABLES + [LATE_TABLE]]
LOOKED_UP = ONE_HOT_TABLES + [LATE_TABLE]
N_ONE_HOT = len(ONE_HOT_TABLES)
N_GATHERED = len(GATHERED_TABLES)
SLOTS = [0] + [n + 1 for n in ONE_HOT_TABLES] + [n + 1 for n in GATHERED_TABLES]

LANES = 4
BLOCKS = -(-N_FEATURES // LANES)
BLOCK_ROWS = [min(LANES * c + LANES - 1, N_FEATURES - 1) for c in range(BLOCKS)]
BLOCK_AT = [sum(BLOCK_ROWS[:c]) for c in range(BLOCKS)]
PAIR_ROWS = sum(BLOCK_ROWS)


def dlrm_tower(nc, dense, ids_gather, ids_one_hot, tables, w_dense, w_pairs, b1, w2, b2, w3, out):
    batch = dense.shape[0]
    tiles = batch // P
    rows = tables[ONE_HOT_TABLES[0]].shape[0]
    KR = 125
    chunks = rows // KR
    SPREAD = KR // 16 * 16
    hidden1 = w_dense.shape[2]
    hidden2 = w2.shape[1]
    n1, n2 = hidden1 // P, hidden2 // P
    assert n1 == 4 and n2 == 2 and tiles == 4
    assert all(tables[n].shape[0] == rows for n in LOOKED_UP) and rows == KR * chunks

    moved = 1 + N_GATHERED
    groups = [range(a, min(a + GATHER_GROUP, moved)) for a in range(0, moved, GATHER_GROUP)]
    NG = len(groups)

    def looked_up_at(t):
        return N_ONE_HOT + (t > 0)

    def features(t, g):
        return [m for m in groups[g] if not (m == 1 and looked_up_at(t) > N_ONE_HOT)]

    def gathers(t, g):
        return sum(len([m for m in features(i, g) if m]) for i in range(t + 1))

    HALF_BATCH = batch // 2
    WHOLE = N_ONE_HOT - 2
    units = [(n, 0, batch) for n in range(WHOLE)]
    units += [(WHOLE, 0, HALF_BATCH), (WHOLE + 1, 0, HALF_BATCH), (WHOLE, HALF_BATCH, HALF_BATCH)]
    units += [(N_ONE_HOT, P, batch - P), (WHOLE + 1, HALF_BATCH, HALF_BATCH)]
    RING = 3

    JOBS = [
        [[("look", 0)], [("move", 0), ("look", 1)], [("move", 1), ("look", 2)], [("move", 2), ("look", 3)],
         [("look", 4), ("move", 3), ("look", 5), ("move", 4), ("move", 5)]],
        [[("look", 6)], [("move", 0)], [("move", 1)], [("move", 2), ("look", 7), ("move", 3)], [("move", 4)],
         [("move", 5)]],
        [[], [("move", 0)], [("move", 1), ("look", 8)], [("move", 2), ("move", 3)], [("move", 4)], [("move", 5)]],
        [[], [("move", 0)], [("move", 1)], [("move", 2), ("move", 3)], [("move", 4)], [("move", 5)]],
    ]
    numbered, count = [], 0
    for parts in JOBS:
        numbered.append([])
        for part in parts:
            banks = 4 if len(numbered) == 1 else 2
            numbered[-1].append([(count + i, (count + i) % banks, kind, what) for i, (kind, what) in enumerate(part)])
            count += len(part)
    job_number = {(at if kind == "move" else 0, kind, what): k
                  for at, parts in enumerate(numbered) for part in parts for k, _, kind, what in part}

    def move_job(t, g):
        return job_number[t, "move", g]

    def look_job(u):
        return job_number[0, "look", u]

    def in_bank(bank, jobs):
        return len([k for parts in numbered for part in parts for k, used, _, _ in part if used == bank and k < jobs])

    def jobs_until(t):
        return sum(len(part) for parts in JOBS[:t + 1] for part in parts)

    SPLIT = [range(0, JQ // 2 + 2), range(JQ // 2 + 2, JQ)]

    def slot(m):
        return 0 if m == 0 else N_ONE_HOT + m

    with ExitStack() as ctx:
        def sb(name, shape, dt=F32):
            return ctx.enter_context(nc.sbuf_tensor(name, shape, dt))

        def psum(name, shape):
            return ctx.enter_context(nc.psum_tensor(name, shape, F32))

        def sem(name):
            return ctx.enter_context(nc.semaphore(name))

        ident = sb("ident", [P, P])
        minus_row = sb("minus_row", [KR, 1])
        idx = sb("idx", [P, tiles, N_GATHERED], I32)
        ids_all = sb("ids_all", [P, len(LOOKED_UP), batch], I32)
        chunk_of = sb("chunk_of", [KR, len(LOOKED_UP), batch])
        table = [sb(f"table{i}", [KR, chunks, P]) for i in range(RING)]
        table_hi = [sb(f"table_hi{i}", [KR, chunks, P], F32R) for i in range(RING)]
        table_lo = [sb(f"table_lo{i}", [KR, chunks, P], F32R) for i in range(RING)]
        one_hot = [sb(f"one_hot{i}", [KR, chunks, batch], F32R) for i in range(RING)]
        looked_up = sb("looked_up", [P, len(LOOKED_UP), batch])
        e = sb("e", [P, moved, P])
        eT = sb("eT", [P, P, PAD])
        gram = sb("gram", [P, LANES * BLOCKS, JQ])
        pairs_t = sb("pairs_t", [P, QUARTERS, PAIR_ROWS])
        pairs = sb("pairs", [PAIR_ROWS, LANES, P])
        wd = sb("wd", [P, 2, hidden1])
        wd_sum = sb("wd_sum", [P, hidden1])
        wp = sb("wp", [PAIR_ROWS, LANES, hidden1])
        w2s = sb("w2s", [P, n1, hidden2])
        w3s = sb("w3s", [P, n2])
        b1s = sb("b1s", [P, n1])
        b2s = sb("b2s", [P, n2])
        h1 = sb("h1", [P, n1, P])
        h2 = sb("h2", [P, n2, P])
        y = sb("y", [1, batch])

        ps_g = [psum(f"ps_g{i}", [P, 512]) for i in range(2)]
        ps_t = [psum(f"ps_t{i}", [P, 4, P]) for i in range(2)]
        ps_x = [psum(f"ps_x{i}", [P, GATHER_GROUP, P]) for i in range(2)] + ps_t
        ps_h = [psum(f"ps_h{i}", [P, 4, P]) for i in range(2)]
        ps_h2 = [ps_h[i][:, 2, :] for i in range(n2)]
        ps_y = ps_h[0][0:1, 3, :]
        ps_z = [ps_g[i][:, 0:2 * P].rearrange("p (q s) -> p q s", q=2) for i in range(2)]

        s_idx = sem("s_idx")
        s_ids_all = [sem(f"s_ids_all{i}") for i in range(len(LOOKED_UP))]
        s_table = [sem(f"s_table{i}") for i in range(len(LOOKED_UP))]
        s_dense = sem("s_dense")
        s_wd = sem("s_wd")
        s_w = sem("s_w")
        s_wd_sum = sem("s_wd_sum")
        s_eT_read = sem("s_eT_read")
        s_gathered = [sem(f"s_gathered{i}") for i in range(NG)]
        s_const = sem("s_const")
        s_chunk_of = sem("s_chunk_of")
        s_chunk_of_first = sem("s_chunk_of_first")
        s_hi = sem("s_hi")
        s_lo = sem("s_lo")
        s_one_hot = sem("s_one_hot")
        s_zero = sem("s_zero")
        s_x = sem("s_x")
        s_emptied = [sem(f"s_emptied{i}") for i in range(4)]
        s_slots = sem("s_slots")
        s_gram = sem("s_gram")
        s_gram_act = sem("s_gram_act")
        s_gram_dve = sem("s_gram_dve")
        s_turn = sem("s_turn")
        s_turn_act = sem("s_turn_act")
        s_turn_dve = sem("s_turn_dve")
        s_pairs = sem("s_pairs")
        s_pairs_act = sem("s_pairs_act")
        s_pairs_dve = sem("s_pairs_dve")
        s_h1 = sem("s_h1")
        s_h1_act = sem("s_h1_act")
        s_h1_dve = sem("s_h1_dve")
        s_h2 = sem("s_h2")
        s_h2_act = sem("s_h2_act")
        s_h2_dve = sem("s_h2_dve")
        s_y = sem("s_y")
        s_y_row = sem("s_y_row")
        s_out = sem("s_out")

        def copies(t, kind, what, bank):
            if kind == "look":
                n, at, samples = units[what]
                return [(looked_up[:, n, at:at + samples], bank.rearrange("p a s -> p (a s)")[:, 0:samples])]
            group = features(t, what)
            at = group[1 if what == 0 else 0]
            last = groups[what][-1] + 1
            parts = [(slot(at), at - groups[what][0], last - groups[what][0])]
            if what == 0:
                parts.append((0, 0, 1))
            return [(eT[:, :, at:at + b - a].rearrange("p s f -> p f s"), bank[:, a:b, :]) for at, a, b in parts]

        block = ctx.enter_context(nc.Block())

        @block.sync
        def _(sp):
            for i, n in enumerate(LOOKED_UP):
                if i >= RING:
                    sp.wait_ge(s_lo, i - RING + 1)
                sp.dma_start(ids_all[:, i, :], ids_one_hot[i].partition_broadcast(P)).then_inc(s_ids_all[i], 16)
                rows_of = tables[n].rearrange("(p c) d -> p c d", c=chunks)
                sp.dma_start(table[i % RING][0:SPREAD], rows_of[0:SPREAD]).then_inc(s_table[i], 16)
                sp.dma_start(table[i % RING][SPREAD:KR], rows_of[SPREAD:KR]).then_inc(s_table[i], 16)
            sp.wait_ge(s_lo, N_ONE_HOT - 2)
            sp.dma_start(wd[:], w_dense.rearrange("s p n -> p s n")).then_inc(s_wd, 16)
            sp.wait_ge(s_lo, N_ONE_HOT)
            sp.dma_start(wp[:], w_pairs.rearrange("a p n -> p a n")).then_inc(s_w, 16)
            sp.dma_start(w2s[:], w2.rearrange("(c p) n -> p c n", p=P)).then_inc(s_w, 16)
            sp.dma_start(w3s[:], w3).then_inc(s_w, 16)
            sp.dma_start(b1s[:], b1).then_inc(s_w, 16)
            sp.dma_start(b2s[:], b2).then_inc(s_w, 16)
            for t in range(1, tiles):
                sp.wait_ge(s_x, move_job(t - 1, 0) + 1)
                sp.dma_start(e[:, 0, :], dense[t * P:(t + 1) * P, :]).then_inc(s_dense, 16)
            sp.wait_ge(s_y_row, tiles)
            sp.dma_start(out.rearrange("b o -> o b"), y[:]).then_inc(s_out, 16)
            sp.wait_ge(s_out, 16)

        @block.gpsimd
        def _(pool):
            pool.memset(ident[:], 0.0).then_inc(s_const, 1)
            pool.iota(minus_row[:], [[0, 1]], base=0, channel_multiplier=-chunks,
                      allow_small_or_imprecise_dtypes=True).then_inc(s_const, 1)
            pool.wait_ge(s_const, 1)
            pool.affine_select(out=ident[:], in_=ident[:], compare_op=ALU.not_equal, fill=1.0, base=0,
                               pattern=[[-1, P]], channel_multiplier=1).then_inc(s_const, 1)
            pool.wait_ge(s_idx, 16)
            for t in range(tiles):
                for g in range(NG):
                    if t:
                        pool.wait_ge(s_x, move_job(t - 1, g) + 1)
                    for m in features(t, g):
                        if m:
                            pool.indirect_dma_start(
                                e[:, m, :], None, tables[GATHERED_TABLES[m - 1]],
                                bass.IndirectOffsetOnAxis(ap=idx[:, t, m - 1:m].bitcast(U32), axis=0),
                            ).then_inc(s_gathered[g], 16)

        @block.scalar
        def _(act):
            def empty(t, part, banks=(0,)):
                for k, bank, kind, what in numbered[t][part]:
                    if bank in banks:
                        act.wait_ge(s_x, k + 1)
                        if kind == "move" and t:
                            act.wait_ge(s_eT_read, t)
                        for out, in_ in copies(t, kind, what, ps_x[bank]):
                            last = act.copy(out, in_)
                        last.then_inc(s_emptied[bank], 1)

            def gram_out(t):
                act.wait_ge(s_gram, 2 * t + 1)
                act.copy(gram[:, 0:N_FEATURES, 0:len(SPLIT[0])].rearrange("p g j -> p j g"),
                         ps_g[0][:, 0:len(SPLIT[0]) * N_FEATURES].rearrange("p (j g) -> p j g", g=N_FEATURES)).then_inc(s_gram_act, 1)

            def turn_out(t):
                act.wait_ge(s_turn, 2 * t + 1)
                for c in range(4):
                    last = act.copy(pairs_t[:, :, BLOCK_AT[c]:BLOCK_AT[c] + BLOCK_ROWS[c]],
                                    ps_t[0][:, c, :].rearrange("p (q f) -> p q f", f=PAD)[:, :, 0:BLOCK_ROWS[c]])
                last.then_inc(s_turn_act, 1)

            def pairs_out(t):
                act.wait_ge(s_pairs, 2 * t + 1)
                act.copy(pairs[:, :, 0:2 * JQ].rearrange("p a (q j) -> p q a j", j=JQ),
                         ps_z[0][0:PAIR_ROWS].rearrange("p q (a j) -> p q a j", j=JQ)).then_inc(s_pairs_act, 1)

            def layer1_out(t):
                act.wait_ge(s_h1, 2 * t + 1)
                for n in range(n1 // 2):
                    act.activation(h1[:, n, :], ps_h[0][:, n, :], ACT.Relu, bias=b1s[:, n:n + 1]).then_inc(s_h1_act, 1)

            def layer2_out(t):
                act.wait_ge(s_h2, 2 * t + 1)
                act.activation(h2[:, 0, :], ps_h2[0], ACT.Relu, bias=b2s[:, 0:1]).then_inc(s_h2_act, 1)

            def chunks_of(n):
                act.wait_ge(s_ids_all[n], 16)
                act.activation(chunk_of[:, n, :], ids_all[0:KR, n, :], ACT.Identity,
                               bias=minus_row[:]).then_inc(s_chunk_of, 1)

            def high_halves(n):
                act.wait_ge(s_table[n], 32)
                if n >= RING:
                    act.wait_ge(s_x, look_job(n - RING) + 1)
                act.activation(table_hi[n % RING][:], table[n % RING][:], ACT.Copy).then_inc(s_hi, 1)

            act.dma_start(idx[:], ids_gather.rearrange("t p f -> p t f")).then_inc(s_idx, 16)
            act.dma_start(e[:, 0, :], dense[0:P, :]).then_inc(s_dense, 16)
            act.wait_ge(s_const, 2)
            high_halves(0)
            chunks_of(1)
            for part in range(len(JOBS[0])):
                high_halves(part + 1)
                chunks_of(part + 2)
                empty(0, part, range(4))
            high_halves(N_ONE_HOT)

            empty(1, 0)

            for t in range(tiles):
                more = t + 1 < tiles
                if t:
                    empty(t, 5)
                gram_out(t)
                turn_out(t)
                pairs_out(t)
                if more:
                    empty(t + 1, 1)
                    empty(t + 1, 2)
                if t == 0:
                    act.wait_ge(s_w, 16 * 5)
                layer1_out(t)
                if more:
                    empty(t + 1, 3)
                layer2_out(t)
                if more:
                    empty(t + 1, 4)

        @block.vector
        def _(dve):
            def empty(t, part):
                for k, bank, kind, what in numbered[t][part]:
                    if bank == 1:
                        dve.wait_ge(s_x, k + 1)
                        if kind == "move":
                            dve.wait_ge(s_eT_read, t)
                        for out, in_ in copies(t, kind, what, ps_x[1]):
                            last = dve.tensor_copy(out, in_)
                        last.then_inc(s_emptied[1], 1)

            def one_hot_rows(u):
                n, at, samples = units[u]
                if u >= RING:
                    dve.wait_ge(s_x, look_job(u - RING) + 1)
                for c in range(chunks):
                    last = dve.tensor_scalar(one_hot[u % RING][:, c, 0:samples], chunk_of[:, n, at:at + samples],
                                             float(c), None, ALU.is_equal)
                last.then_inc(s_one_hot, 1)

            def low_halves(n):
                dve.wait_ge(s_hi, n + 1)
                dve.tensor_tensor(table_lo[n % RING][:], table[n % RING][:], table_hi[n % RING][:].bitcast(F32),
                                  ALU.subtract).then_inc(s_lo, 1)

            def one_hot_slots(t):
                done = max(look_job(u) for u, (_, at, _) in enumerate(units) if at <= t * P) + 1
                for bank in range(4):
                    dve.wait_ge(s_emptied[bank], in_bank(bank, done))
                if t:
                    dve.wait_ge(s_eT_read, t)
                dve.tensor_copy(eT[:, :, 1:1 + looked_up_at(t)].rearrange("p s f -> p f s"),
                                looked_up[:, 0:looked_up_at(t), t * P:(t + 1) * P]).then_inc(s_slots, 1)

            def gram_out(t):
                dve.wait_ge(s_gram, 2 * t + 2)
                dve.tensor_copy(gram[:, 0:N_FEATURES, len(SPLIT[0]):JQ].rearrange("p g j -> p j g"),
                                ps_g[1][:, 0:len(SPLIT[1]) * N_FEATURES].rearrange("p (j g) -> p j g", g=N_FEATURES)).then_inc(s_gram_dve, 1)

            def turn_out(t):
                dve.wait_ge(s_turn, 2 * t + 2)
                for c in range(4, BLOCKS):
                    last = dve.tensor_copy(pairs_t[:, :, BLOCK_AT[c]:BLOCK_AT[c] + BLOCK_ROWS[c]],
                                           ps_t[1][:, c - 4, :].rearrange("p (q f) -> p q f", f=PAD)[:, :, 0:BLOCK_ROWS[c]])
                last.then_inc(s_turn_dve, 1)

            def pairs_out(t):
                dve.wait_ge(s_pairs, 2 * t + 2)
                dve.tensor_copy(pairs[:, :, 2 * JQ:4 * JQ].rearrange("p a (q j) -> p q a j", j=JQ),
                                ps_z[1][0:PAIR_ROWS].rearrange("p q (a j) -> p q a j", j=JQ)).then_inc(s_pairs_dve, 1)

            def layer1_out(t):
                dve.wait_ge(s_h1, 2 * t + 2)
                for n in range(n1 // 2, n1):
                    dve.tensor_scalar(h1[:, n, :], ps_h[1][:, n - n1 // 2, :], b1s[:, n:n + 1], 0.0,
                                      ALU.add, ALU.max).then_inc(s_h1_dve, 1)

            def layer2_out(t):
                dve.wait_ge(s_h2, 2 * t + 2)
                dve.tensor_scalar(h2[:, 1, :], ps_h2[1], b2s[:, 1:2], 0.0, ALU.add, ALU.max).then_inc(s_h2_dve, 1)

            def output_out(t):
                dve.wait_ge(s_y, t + 1)
                dve.tensor_copy(y[0:1, t * P:(t + 1) * P], ps_y).then_inc(s_y_row, 1)

            dve.memset(eT[:, :, N_FEATURES:PAD], 0.0).then_inc(s_zero, 1)
            dve.memset(gram[:, N_FEATURES:LANES * BLOCKS, :], 0.0).then_inc(s_zero, 1)
            for n in range(N_ONE_HOT):
                if n:
                    dve.wait_ge(s_chunk_of, n)
                else:
                    dve.wait_ge(s_const, 2)
                    dve.wait_ge(s_ids_all[0], 16)
                    dve.tensor_scalar(chunk_of[:, 0, :], ids_all[0:KR, 0, :], minus_row[:], None,
                                      ALU.add).then_inc(s_chunk_of_first, 1)
                    dve.wait_ge(s_chunk_of_first, 1)
                one_hot_rows(n)
                low_halves(n)
            one_hot_rows(N_ONE_HOT)
            one_hot_slots(0)
            dve.wait_ge(s_wd, 16)
            dve.tensor_tensor(wd_sum[:], wd[:, 0, :], wd[:, 1, :], ALU.add).then_inc(s_wd_sum, 1)
            dve.wait_ge(s_chunk_of, N_ONE_HOT)
            one_hot_rows(N_ONE_HOT + 1)
            low_halves(N_ONE_HOT)
            one_hot_rows(N_ONE_HOT + 2)

            empty(1, 0)
            for t in range(tiles):
                more = t + 1 < tiles
                if t:
                    empty(t, 5)
                    output_out(t - 1)
                gram_out(t)
                turn_out(t)
                pairs_out(t)
                if more:
                    empty(t + 1, 1)
                    empty(t + 1, 2)
                if t == 0:
                    dve.wait_ge(s_w, 16 * 5)
                layer1_out(t)
                if more:
                    empty(t + 1, 3)
                layer2_out(t)
                if more:
                    one_hot_slots(t + 1)
                    empty(t + 1, 4)
            output_out(tiles - 1)

        @block.tensor
        def _(pe):
            def run(t, part):
                for k, bank, kind, what in numbered[t][part]:
                    if in_bank(bank, k):
                        pe.wait_ge(s_emptied[bank], in_bank(bank, k))
                    if kind == "look":
                        n, _, samples = units[what]
                        pe.wait_ge(s_one_hot, what + 1)
                        for half, s_half in ((table_hi, s_hi), (table_lo, s_lo)):
                            pe.wait_ge(s_half, n + 1)
                            for c in range(chunks):
                                last = pe.matmul(ps_x[bank][:].rearrange("p a s -> p (a s)")[:, 0:samples],
                                                 half[n % RING][:, c, :], one_hot[what % RING][:, c, 0:samples],
                                                 start=(half is table_hi and c == 0),
                                                 stop=(half is table_lo and c == chunks - 1))
                    else:
                        if what == 0:
                            pe.wait_ge(s_dense, 16 * t + 16)
                        pe.wait_ge(s_gathered[what], 16 * gathers(t, what))
                        for m in features(t, what):
                            last = pe.transpose(ps_x[bank][:, m - groups[what][0], :], e[:, m, :], ident[:])
                    last.then_inc(s_x, 1)

            def keep_busy(products):
                for _ in range(products):
                    pe.matmul(ps_g[0][:, 0:P], ident[:], ident[:], start=True, stop=True)

            def grams(t, half):
                if half == 0:
                    for bank in range(4):
                        pe.wait_ge(s_emptied[bank], in_bank(bank, jobs_until(t)))
                    pe.wait_ge(s_slots, t + 1)
                    if t:
                        pe.wait_ge(s_pairs_act, t)
                        pe.wait_ge(s_pairs_dve, t)
                for j in range(len(SPLIT[half])):
                    for q in range(QUARTERS):
                        s = q * JQ + SPLIT[half][j]
                        last = pe.matmul(ps_g[half][q * PAD:(q + 1) * PAD, j * N_FEATURES:(j + 1) * N_FEATURES],
                                         eT[:, s, :], eT[:, s, 0:N_FEATURES], start=True, stop=True,
                                         tile_position=(0, q * PAD))
                last.then_inc(s_gram, 1)

            def dense_part(t, half):
                if t and half == 0:
                    pe.wait_ge(s_y_row, t)
                for n in range(2 * half, 2 * half + 2):
                    last = pe.matmul(ps_h[n // 2][:, n % 2, :], wd_sum[:, n * P:(n + 1) * P], eT[:, :, 0],
                                     start=(n % 2 == 0), stop=False, skip_group_check=True)
                if half == 1:
                    last.then_inc(s_eT_read, 1)

            def turn(t):
                pe.wait_ge(s_gram_act, t + 1)
                pe.wait_ge(s_gram_dve, t + 1)
                for c in range(BLOCKS):
                    last = pe.transpose(ps_t[c // 4][:, c % 4, :],
                                        gram[:, LANES * c:LANES * c + LANES, :].rearrange("p g j -> p (g j)"), ident[:])
                    if c in (3, BLOCKS - 1):
                        last.then_inc(s_turn, 1)

            def pair_turn(t):
                pe.wait_ge(s_turn_act, t + 1)
                pe.wait_ge(s_turn_dve, t + 1)
                for q in range(QUARTERS):
                    last = pe.transpose(ps_z[q // 2][0:PAIR_ROWS, q % 2, :], pairs_t[:, q, :], ident[:])
                    if q % 2:
                        last.then_inc(s_pairs, 1)

            def layer1(t, half):
                if half == 0:
                    pe.wait_ge(s_pairs_act, t + 1)
                    pe.wait_ge(s_pairs_dve, t + 1)
                for n in range(2 * half, 2 * half + 2):
                    for a in range(LANES):
                        last = pe.matmul(ps_h[half][:, n % 2, :], wp[:, a, n * P:(n + 1) * P], pairs[:, a, :],
                                         start=False, stop=(a == LANES - 1), skip_group_check=True)
                last.then_inc(s_h1, 1)

            def layer2(t, n):
                for k in range(n1):
                    if n == 0 and k == 0:
                        pe.wait_ge(s_h1_act, 2 * t + 2)
                    elif n == 0 and k >= 2:
                        pe.wait_ge(s_h1_dve, 2 * t + k - 1)
                    last = pe.matmul(ps_h2[n], w2s[:, k, n * P:(n + 1) * P], h1[:, k, :],
                                     start=(k == 0), stop=(k == n1 - 1))
                last.then_inc(s_h2, 1)

            def layer3(t):
                for n, s_half in enumerate((s_h2_act, s_h2_dve)):
                    pe.wait_ge(s_half, t + 1)
                    last = pe.matmul(ps_y, w3s[:, n:n + 1], h2[:, n, :], start=(n == 0), stop=(n == n2 - 1))
                last.then_inc(s_y, 1)

            pe.wait_ge(s_const, 3)
            keep_busy(14)
            for part in range(len(JOBS[0])):
                run(0, part)
            run(1, 0)

            for t in range(tiles):
                more = t + 1 < tiles
                if t:
                    run(t, 5)
                    layer3(t - 1)
                grams(t, 0)
                grams(t, 1)
                if t == 0:
                    pe.wait_ge(s_wd_sum, 1)
                dense_part(t, 0)
                if t == 0:
                    pe.wait_ge(s_zero, 2)
                turn(t)
                dense_part(t, 1)
                pair_turn(t)
                if more:
                    run(t + 1, 1)
                    run(t + 1, 2)
                if t == 0:
                    pe.wait_ge(s_w, 16 * 5)
                layer1(t, 0)
                layer1(t, 1)
                if more:
                    run(t + 1, 3)
                layer2(t, 0)
                layer2(t, 1)
                if t == tiles - 2:
                    keep_busy(9)
                if more:
                    run(t + 1, 4)
            layer3(tiles - 1)


def kernel(**inputs):
    import numpy as np
    import concourse.bacc as bacc
    from concourse.bass_utils import run_bass_kernel_spmd

    nc = bacc.Bacc("TRN2", target_bir_lowering=False, num_devices=1)
    given = {name: np.asarray(a) for name, a in inputs.items()}
    batch = given["ids"].shape[0]

    w1 = given["W_top1"]
    zero_row = w1.shape[0]
    row_of, at = {}, P
    for i in range(N_FEATURES):
        for j in range(i + 1, N_FEATURES):
            row_of[i, j] = at
            at += 1
    order = np.full((LANES, PAIR_ROWS), zero_row)
    for a in range(LANES):
        for c in range(BLOCKS):
            g = LANES * c + a
            for f in range(min(g, N_FEATURES - 1) if g < N_FEATURES else 0):
                order[a, BLOCK_AT[c] + f] = row_of[min(SLOTS[f], SLOTS[g]), max(SLOTS[f], SLOTS[g])]
    w1_padded = np.concatenate([w1, np.zeros((1, w1.shape[1]), w1.dtype)])

    arrays = {
        "dense": given["r_dense_features"],
        "ids_gather": given["ids"][:, GATHERED_TABLES].reshape(batch // P, P, N_GATHERED),
        "ids_one_hot": given["ids"].T[LOOKED_UP],
        "w_dense": np.stack([w1[:P], w1[-P:]]),
        "w_pairs": w1_padded[order],
        "b1": given["b_top1"].reshape(-1, P).T,
        "w2": given["W_top2"],
        "b2": given["b_top2"].reshape(-1, P).T,
        "w3": given["W_top3"].reshape(-1, P).T,
    }
    arrays.update({f"tbl_{n}": given[f"tbl_{n}"] for n in range(N_TABLES)})
    arrays = {name: np.ascontiguousarray(a) for name, a in arrays.items()}
    ap = {name: nc.dram_tensor(name, a.shape, mybir.dt.from_np(a.dtype), kind="ExternalInput").ap()
          for name, a in arrays.items()}
    out = nc.dram_tensor("y_out", (batch, 1), F32, kind="ExternalOutput").ap()
    dlrm_tower(nc, ap["dense"], ap["ids_gather"], ap["ids_one_hot"], [ap[f"tbl_{n}"] for n in range(N_TABLES)],
               ap["w_dense"], ap["w_pairs"], ap["b1"], ap["w2"], ap["b2"], ap["w3"], out)
    r = run_bass_kernel_spmd(nc, [arrays], core_ids=[0])
    return r.results[0]["y_out"]
```
